# Optimizing a Trainium2 kernel written in Bass

```python
import numpy as np
import jax
import jax.numpy as jnp

def _softmax(x, axis=-1):
    return jax.nn.softmax(x, axis=axis)

def _gelu(x):
    return jax.nn.gelu(x, approximate=True)

def _silu(x):
    return jax.nn.silu(x)

def _sigmoid(x):
    return jax.nn.sigmoid(x)

def _layernorm(x, axis=-1, eps=1e-05):
    m = jnp.mean(x, axis=axis, keepdims=True)
    v = jnp.var(x, axis=axis, keepdims=True)
    return (x - m) / jnp.sqrt(v + eps)

def _scatter_add(tgt, idx, src, axis=0):
    return tgt.at[idx].add(src)

def _segment_sum(src, seg, n):
    return jax.ops.segment_sum(src, seg, n)
kernel_name = 'mk_sandwich_d2_jaxref_r4_bbf901'

def setup_inputs(seed: int=0):
    np.random.seed(seed)
    _w = jnp.asarray

    def _L0_attn_setup():
        import jax, jax.numpy as jnp
        import numpy as np
        B, T, C = (4, 512, 256)

        def wkv(k, v, w, u, reverse):

            def step(carry, kv):
                num, den, mx = carry
                k_t, v_t = kv
                ku = k_t + u
                m = jnp.maximum(mx, ku)
                e1 = jnp.exp(mx - m)
                e2 = jnp.exp(ku - m)
                y = (e1 * num + e2 * v_t) / (e1 * den + e2)
                mw = mx + w
                mn = jnp.maximum(mw, k_t)
                e1s = jnp.exp(mw - mn)
                e2s = jnp.exp(k_t - mn)
                return ((e1s * num + e2s * v_t, e1s * den + e2s, mn), y)
            z = jnp.zeros_like(k[:, 0])
            init = (z, z, jnp.full_like(z, -1e+38))
            ks = jnp.swapaxes(k, 0, 1)
            vs = jnp.swapaxes(v, 0, 1)
            _, ys = jax.lax.scan(step, init, (ks, vs), reverse=reverse)
            return jnp.swapaxes(ys, 0, 1)
        key = jax.random.key(seed)
        k1, k2, k3, k4, k5, k6, k7 = jax.random.split(key, 7)
        x = jax.random.normal(k1, (B, T, C), dtype=jnp.float32)
        rkv_w = jax.random.normal(k2, (6 * C, C), dtype=jnp.float32) / np.sqrt(C)
        out_w = jax.random.normal(k3, (C, 2 * C), dtype=jnp.float32) / np.sqrt(2 * C)
        time_decay = jax.random.uniform(k4, (C,), jnp.float32, -6.0, -5.0)
        time_first = jax.random.uniform(k5, (C,), jnp.float32, -3.0, 0.0)
        time_decay_rev = jax.random.uniform(k6, (C,), jnp.float32, -6.0, -5.0)
        time_first_rev = jax.random.uniform(k7, (C,), jnp.float32, -3.0, 0.0)
        return {'x': x, 'rkv_w': rkv_w, 'out_w': out_w, 'time_decay': time_decay, 'time_first': time_first, 'time_decay_rev': time_decay_rev, 'time_first_rev': time_first_rev}
    _L0_attn_in = _L0_attn_setup()

    def _L0_ffn_setup():
        import jax, jax.numpy as jnp
        import numpy as np
        B, S, D, E, H, K = (64, 512, 256, 32, 1024, 8)
        key = jax.random.key(seed)
        k0, k1, k2, k3 = jax.random.split(key, 4)
        x = jax.random.normal(k0, (B, S, D), jnp.float32)
        gate_w = jax.random.normal(k1, (E, D), jnp.float32) * (1.0 / np.sqrt(D))
        gate_b = jnp.zeros((E,), jnp.float32)
        w1 = jax.random.normal(k2, (E, D + 1, H), jnp.float32) * (1.0 / np.sqrt(D + 1))
        w2 = jax.random.normal(k3, (E, H + 1, D), jnp.float32) * (1.0 / np.sqrt(H + 1))
        return {'x': x, 'gate_w': gate_w, 'gate_b': gate_b, 'w1': w1, 'w2': w2}
    _L0_ffn_in = _L0_ffn_setup()

    def _L1_attn_setup():
        import jax, jax.numpy as jnp
        import numpy as np
        HIDDEN = 256
        N_HEAD = 16
        HEAD_DIM = HIDDEN // N_HEAD
        BATCH = 1
        SEQ = 1024
        THETA = 10000.0

        def _rope_cos_sin(seq_len, head_dim, dtype=jnp.float32):
            inv_freq = 1.0 / THETA ** (jnp.arange(0, head_dim, 2, dtype=dtype) / head_dim)
            t = jnp.arange(seq_len, dtype=dtype)
            freqs = jnp.outer(t, inv_freq)
            return (jnp.cos(freqs), jnp.sin(freqs))

        def _apply_rope(x, cos, sin):
            x2 = x.reshape(*x.shape[:-1], -1, 2)
            x_re, x_im = (x2[..., 0], x2[..., 1])
            c = cos[None, :, None, :]
            s = sin[None, :, None, :]
            out_re = x_re * c - x_im * s
            out_im = x_re * s + x_im * c
            out = jnp.stack([out_re, out_im], axis=-1)
            return out.reshape(x.shape)
        key = jax.random.key(seed)
        kx, kq, kk, kv = jax.random.split(key, 4)
        scale = 1.0 / np.sqrt(HIDDEN)
        return {'x': jax.random.normal(kx, (BATCH, SEQ, HIDDEN), dtype=jnp.float32), 'wq': jax.random.normal(kq, (HIDDEN, HIDDEN), dtype=jnp.float32) * scale, 'wk': jax.random.normal(kk, (HIDDEN, HIDDEN), dtype=jnp.float32) * scale, 'wv': jax.random.normal(kv, (HIDDEN, HIDDEN), dtype=jnp.float32) * scale}
    _L1_attn_in = _L1_attn_setup()

    def _L1_ffn_setup():
        import jax, jax.numpy as jnp
        import numpy as np
        B, T, D, E, H = (4, 512, 256, 4, 8)
        EPS = 1e-05

        def _uniform(k, shape, bound):
            return jax.random.uniform(k, shape, jnp.float32, -bound, bound)

        def _layernorm(x, w, b):
            mu = jnp.mean(x, axis=-1, keepdims=True)
            var = jnp.mean(jnp.square(x - mu), axis=-1, keepdims=True)
            return (x - mu) * jax.lax.rsqrt(var + EPS) * w + b
        key = jax.random.key(seed)
        ks = jax.random.split(key, 12)
        wb = np.sqrt(6.0 / D) / np.sqrt(6.0)
        wb = 1.0 / np.sqrt(D)
        return {'x': jax.random.normal(ks[0], (B, T, D), jnp.float32), 'router_prob': jax.random.uniform(ks[1], (B, T, E), jnp.float32), 'norm_w': jnp.ones((D,), jnp.float32), 'norm_b': jnp.zeros((D,), jnp.float32), 'q_w': _uniform(ks[2], (D, D), wb), 'q_b': _uniform(ks[3], (D,), wb), 'k_w': _uniform(ks[4], (D, D), wb), 'k_b': _uniform(ks[5], (D,), wb), 'v_w': _uniform(ks[6], (D, D), wb), 'v_b': _uniform(ks[7], (D,), wb), 'o_w': _uniform(ks[8], (D, D), wb), 'o_b': _uniform(ks[9], (D,), wb)}
    _L1_ffn_in = _L1_ffn_setup()
    _d = {'L0_attn_x': _L0_attn_in['x'], 'L0_attn_rkv_w': _L0_attn_in['rkv_w'], 'L0_attn_out_w': _L0_attn_in['out_w'], 'L0_attn_time_decay': _L0_attn_in['time_decay'], 'L0_attn_time_first': _L0_attn_in['time_first'], 'L0_attn_time_decay_rev': _L0_attn_in['time_decay_rev'], 'L0_attn_time_first_rev': _L0_attn_in['time_first_rev'], 'L0_ffn_gate_w': _L0_ffn_in['gate_w'], 'L0_ffn_gate_b': _L0_ffn_in['gate_b'], 'L0_ffn_w1': _L0_ffn_in['w1'], 'L0_ffn_w2': _L0_ffn_in['w2'], 'L1_attn_wq': _L1_attn_in['wq'], 'L1_attn_wk': _L1_attn_in['wk'], 'L1_attn_wv': _L1_attn_in['wv'], 'L1_ffn_router_prob': _L1_ffn_in['router_prob'], 'L1_ffn_norm_w': _L1_ffn_in['norm_w'], 'L1_ffn_norm_b': _L1_ffn_in['norm_b'], 'L1_ffn_q_w': _L1_ffn_in['q_w'], 'L1_ffn_q_b': _L1_ffn_in['q_b'], 'L1_ffn_k_w': _L1_ffn_in['k_w'], 'L1_ffn_k_b': _L1_ffn_in['k_b'], 'L1_ffn_v_w': _L1_ffn_in['v_w'], 'L1_ffn_v_b': _L1_ffn_in['v_b'], 'L1_ffn_o_w': _L1_ffn_in['o_w'], 'L1_ffn_o_b': _L1_ffn_in['o_b']}
    _x0 = _d['L0_attn_x']
    _d['L0_attn_x'] = jax.random.normal(jax.random.fold_in(jax.random.key(seed), 1), (4, 2048, 256), dtype=_x0.dtype)
    del _x0
    return _d

def reference(L0_attn_x, L0_attn_rkv_w, L0_attn_out_w, L0_attn_time_decay, L0_attn_time_first, L0_attn_time_decay_rev, L0_attn_time_first_rev, L0_ffn_gate_w, L0_ffn_gate_b, L0_ffn_w1, L0_ffn_w2, L1_attn_wq, L1_attn_wk, L1_attn_wv, L1_ffn_router_prob, L1_ffn_norm_w, L1_ffn_norm_b, L1_ffn_q_w, L1_ffn_q_b, L1_ffn_k_w, L1_ffn_k_b, L1_ffn_v_w, L1_ffn_v_b, L1_ffn_o_w, L1_ffn_o_b):

    def _L0_attn_ref(x, rkv_w, out_w, time_decay, time_first, time_decay_rev, time_first_rev):
        import jax, jax.numpy as jnp
        import numpy as np
        B, T, C = (4, 512, 256)

        def wkv(k, v, w, u, reverse):

            def step(carry, kv):
                num, den, mx = carry
                k_t, v_t = kv
                ku = k_t + u
                m = jnp.maximum(mx, ku)
                e1 = jnp.exp(mx - m)
                e2 = jnp.exp(ku - m)
                y = (e1 * num + e2 * v_t) / (e1 * den + e2)
                mw = mx + w
                mn = jnp.maximum(mw, k_t)
                e1s = jnp.exp(mw - mn)
                e2s = jnp.exp(k_t - mn)
                return ((e1s * num + e2s * v_t, e1s * den + e2s, mn), y)
            z = jnp.zeros_like(k[:, 0])
            init = (z, z, jnp.full_like(z, -1e+38))
            ks = jnp.swapaxes(k, 0, 1)
            vs = jnp.swapaxes(v, 0, 1)
            _, ys = jax.lax.scan(step, init, (ks, vs), reverse=reverse)
            return jnp.swapaxes(ys, 0, 1)
        b, t, c = x.shape
        rkv = jnp.einsum('btc,dc->btd', x, rkv_w).reshape(b, t, 2, 3, c)
        r_f, k_f, v_f = (rkv[:, :, 0, 0], rkv[:, :, 0, 1], rkv[:, :, 0, 2])
        r_b, k_b, v_b = (rkv[:, :, 1, 0], rkv[:, :, 1, 1], rkv[:, :, 1, 2])
        out_f = jax.nn.sigmoid(r_f) * wkv(k_f, v_f, -jnp.exp(time_decay), time_first, False)
        out_b = jax.nn.sigmoid(r_b) * wkv(k_b, v_b, -jnp.exp(time_decay_rev), time_first_rev, True)
        out_cat = jnp.concatenate([out_f, out_b], axis=-1)
        return jnp.einsum('btd,cd->btc', out_cat, out_w)

    def _L0_ffn_ref(x, gate_w, gate_b, w1, w2):
        import jax, jax.numpy as jnp
        import numpy as np
        B, S, D, E, H, K = (64, 512, 256, 32, 1024, 8)
        b, s, d = x.shape
        logits = jnp.einsum('bsd,ed->bse', x, gate_w) + gate_b
        probs = jax.nn.softmax(logits, axis=-2)
        vals_t, idx_t = jax.lax.top_k(probs.transpose(0, 2, 1), K)
        vals = vals_t.transpose(0, 2, 1)
        idx = idx_t.transpose(0, 2, 1)
        flat_idx = idx.reshape(b, K * E)
        tok = jnp.take_along_axis(x, flat_idx[:, :, None], axis=1)
        tok = tok.reshape(b, K, E, d)
        merged = jnp.einsum('bked,bke->bed', tok, vals)
        ones = jnp.ones(merged.shape[:-1] + (1,), merged.dtype)
        h = jnp.einsum('bei,eih->beh', jnp.concatenate([merged, ones], -1), w1)
        h = jax.nn.gelu(h, approximate=False)
        o = jnp.einsum('bej,ejo->beo', jnp.concatenate([h, ones], -1), w2)
        out_tok = jnp.einsum('beo,bke->bkeo', o, vals).reshape(b, K * E, d)
        out = jnp.zeros_like(x).at[jnp.arange(b)[:, None], flat_idx].add(out_tok)
        return out

    def _L1_attn_ref(x, wq, wk, wv):
        import jax, jax.numpy as jnp
        import numpy as np
        HIDDEN = 256
        N_HEAD = 16
        HEAD_DIM = HIDDEN // N_HEAD
        BATCH = 1
        SEQ = 1024
        THETA = 10000.0

        def _rope_cos_sin(seq_len, head_dim, dtype=jnp.float32):
            inv_freq = 1.0 / THETA ** (jnp.arange(0, head_dim, 2, dtype=dtype) / head_dim)
            t = jnp.arange(seq_len, dtype=dtype)
            freqs = jnp.outer(t, inv_freq)
            return (jnp.cos(freqs), jnp.sin(freqs))

        def _apply_rope(x, cos, sin):
            x2 = x.reshape(*x.shape[:-1], -1, 2)
            x_re, x_im = (x2[..., 0], x2[..., 1])
            c = cos[None, :, None, :]
            s = sin[None, :, None, :]
            out_re = x_re * c - x_im * s
            out_im = x_re * s + x_im * c
            out = jnp.stack([out_re, out_im], axis=-1)
            return out.reshape(x.shape)
        B, S, _ = x.shape
        xq = (x @ wq.T).reshape(B, S, N_HEAD, HEAD_DIM).astype(jnp.float32)
        xk = (x @ wk.T).reshape(B, S, N_HEAD, HEAD_DIM).astype(jnp.float32)
        xv = (x @ wv.T).reshape(B, S, N_HEAD, HEAD_DIM).astype(jnp.float32)
        cos, sin = _rope_cos_sin(S, HEAD_DIM)
        q = _apply_rope(xq, cos, sin)
        k = _apply_rope(xk, cos, sin)
        scores = jnp.einsum('bqhd,bkhd->bhqk', q, k) / jnp.sqrt(jnp.asarray(HEAD_DIM, dtype=q.dtype))
        attn = jax.nn.softmax(scores, axis=-1)
        out = jnp.einsum('bhqk,bkhd->bqhd', attn, xv)
        return out.reshape(B, S, N_HEAD * HEAD_DIM)

    def _L1_ffn_ref(x, router_prob, norm_w, norm_b, q_w, q_b, k_w, k_b, v_w, v_b, o_w, o_b):
        import jax, jax.numpy as jnp
        import numpy as np
        B, T, D, E, H = (4, 512, 256, 4, 8)
        EPS = 1e-05

        def _uniform(k, shape, bound):
            return jax.random.uniform(k, shape, jnp.float32, -bound, bound)

        def _layernorm(x, w, b):
            mu = jnp.mean(x, axis=-1, keepdims=True)
            var = jnp.mean(jnp.square(x - mu), axis=-1, keepdims=True)
            return (x - mu) * jax.lax.rsqrt(var + EPS) * w + b
        e_cnt = router_prob.shape[2]
        b, t, d = x.shape
        n = t // e_cnt
        h = H
        scale = d ** (-0.5)
        qs, ks_, vs = ([], [], [])
        for e in range(e_cnt):
            xe = x[:, e * n:(e + 1) * n, :]
            xn = _layernorm(xe, norm_w, norm_b)
            m = d // 2 ** e
            xm = xn[..., :m]
            qs.append(jnp.einsum('bnm,dm->bnd', xm, q_w[:, :m]) + q_b)
            ks_.append(jnp.einsum('bnm,dm->bnd', xm, k_w[:, :m]) + k_b)
            vs.append(jnp.einsum('bnm,dm->bnd', xm, v_w[:, :m]) + v_b)
        q = jnp.concatenate(qs, axis=1)
        k = jnp.concatenate(ks_, axis=1)
        v = jnp.concatenate(vs, axis=1)
        dh = d // h
        q = q.reshape(b, t, h, dh).transpose(0, 2, 1, 3)
        k = k.reshape(b, t, h, dh).transpose(0, 2, 1, 3)
        v = v.reshape(b, t, h, dh).transpose(0, 2, 1, 3)
        attn = jnp.einsum('bhqd,bhkd->bhqk', q, k) * scale
        attn = jax.nn.softmax(attn, axis=-1)
        attn_out = jnp.einsum('bhqk,bhkd->bhqd', attn, v)
        attn_out = attn_out.transpose(0, 2, 1, 3).reshape(b, t, d)
        outs = []
        for e in range(e_cnt):
            sl = slice(e * n, (e + 1) * n)
            m = d // 2 ** e
            xm = attn_out[:, sl, :m]
            out = jnp.einsum('bnm,om->bno', xm, o_w[:m, :m]) + o_b[:m]
            pad = d - m
            if pad:
                out = jnp.pad(out, ((0, 0), (0, 0), (0, pad)))
            outs.append(out + x[:, sl, :])
        return jnp.concatenate(outs, axis=1)
    x = L0_attn_x
    x = x + _layernorm(_L0_attn_ref(_layernorm(x, axis=-1), L0_attn_rkv_w, L0_attn_out_w, L0_attn_time_decay, L0_attn_time_first, L0_attn_time_decay_rev, L0_attn_time_first_rev), axis=-1)
    x = x + _layernorm(_L0_ffn_ref(_layernorm(x, axis=-1), L0_ffn_gate_w, L0_ffn_gate_b, L0_ffn_w1, L0_ffn_w2), axis=-1)
    x = x + _layernorm(_L1_attn_ref(_layernorm(x, axis=-1), L1_attn_wq, L1_attn_wk, L1_attn_wv), axis=-1)
    x = x + _layernorm(_L1_ffn_ref(_layernorm(x, axis=-1), L1_ffn_router_prob, L1_ffn_norm_w, L1_ffn_norm_b, L1_ffn_q_w, L1_ffn_q_b, L1_ffn_k_w, L1_ffn_k_b, L1_ffn_v_w, L1_ffn_v_b, L1_ffn_o_w, L1_ffn_o_b), axis=-1)
    return x

_drawn_inputs = setup_inputs


def setup_inputs(seed=0):
    import zlib

    import numpy as np

    out = dict(_drawn_inputs(seed))
    spreads = {'L0_ffn_gate_b': (0.0, 2.0), 'L1_ffn_norm_w': (1.0, 0.6), 'L1_ffn_norm_b': (0.0, 0.8)}
    factors = {'L0_attn_time_first': 48.098,
     'L0_attn_time_first_rev': 40.612,
     'L1_ffn_q_w': 8.0,
     'L1_ffn_q_b': 62.871,
     'L1_ffn_k_w': 8.0,
     'L1_ffn_k_b': 64.0,
     'L1_ffn_v_b': 8.0,
     'L1_ffn_o_b': 6.043}
    for name, (base, spread) in spreads.items():
        noise = np.random.default_rng([zlib.crc32(name.encode()), seed]).standard_normal(out[name].shape)
        drawn = base * np.exp(spread * noise) if base else spread * noise
        out[name] = jnp.asarray(drawn.astype(out[name].dtype))
    for name, factor in factors.items():
        out[name] = (out[name] * factor).astype(out[name].dtype)
    return out
```

```python
from contextlib import ExitStack

import concourse.bass as bass
from concourse import mybir

F32 = mybir.dt.float32
F32R = mybir.dt.float32r
ALU = mybir.AluOpType
ACT = mybir.ActivationFunctionType
AX_X = mybir.AxisListType.X

P = 128
B, T, D = 4, 2048, 256
TOK = B * T
GT = 512
J = GT // P
NG = TOK // GT
CC = D // P
EPS = 1e-5


def wait(eng, sem, value, step=None):
    if isinstance(value, int):
        if value > 0:
            eng.wait_ge(sem, value)
        return
    eng.wait_ge(sem, value)
    if step is not None:
        eng.sem_inc(step, 1)


def peeled(eng, n, body, last=False):
    body(0)
    end = n - 1 if last else n
    if end > 1:
        with eng.Fori(1, end) as i:
            body(i)
    if last:
        body(n - 1)


def following(b, e, n):
    if e + 1 < n:
        return b, e + 1
    return None if isinstance(b, int) and b == B - 1 else (b + 1, 0)


class Chain:

    def __init__(self, eng, sem, per_round, step=None):
        self.eng, self.sem, self.per, self.step = eng, sem, per_round, step
        self.i, self.k = 0, 0

    def start(self, i):
        self.i, self.k = i, 0

    def mark(self, ins):
        self.k += 1
        assert self.k <= self.per
        ins.then_inc(self.sem, 1)

    def settle(self, apart=False):
        wait(self.eng, self.sem, self.i * self.per + self.k, self.step if apart else None)

    def link(self, ins, apart=False):
        self.mark(ins)
        self.settle(apart)

    def end(self):
        assert self.k == self.per, self.k


class Mem:

    def __init__(self, nc, ctx, tag):
        self.nc, self.ctx, self.tag, self.sems = nc, ctx, tag, []
        ctx.callback(self.clear)

    def clear(self):
        self.nc.clear_and_free_semaphores(self.sems)
        self.nc.all_engine_barrier()

    def sb(self, name, shape, dt=F32):
        return self.ctx.enter_context(self.nc.sbuf_tensor(f"{self.tag}_{name}", shape, dt))

    def ps(self, name, shape, dt=F32):
        return self.ctx.enter_context(self.nc.psum_tensor(f"{self.tag}_{name}", shape, dt))

    def sem(self, name):
        self.sems.append(self.nc.alloc_semaphore(name=f"{self.tag}_{name}"))
        return self.sems[-1]


def group(v, g):
    if isinstance(g, int):
        return v[g]
    n = len(v.shape)
    axes = " ".join("abcdef"[:n - 1])
    return v[bass.ds(g, 1)].rearrange(f"o {axes} -> (o a) {' '.join('abcdef'[1:n - 1])}")


def tokens(ap):
    return ap.rearrange("(g j p) n -> g p j n", j=J, p=P)


LN_LINKS = 2


def ln_stats(nc, ch, src, stats, mv, var_ready):
    for j in range(J):
        ins = nc.vector.bn_stats(stats[:, j, :], src[:, j, :])
    ch.link(ins, apart=True)
    for j in range(J):
        ins = nc.vector.bn_aggr(mv[:, j, :], stats[:, j, :])
    ins.then_inc(var_ready, 1)


def ln_rstd(nc, ch, mv, veps, rstd, nhalf, rstd_ready):
    ch.link(nc.gpsimd.tensor_scalar(veps[:, :], mv[:, :, 1], EPS, None, ALU.add))
    nc.gpsimd.tensor_tensor(rstd[:, :], veps[:, :], nhalf[:, :], ALU.pow).then_inc(rstd_ready, 1)


def ln_apply(nc, src, mv, rstd, dst):
    for j in range(J):
        ins = nc.vector.tensor_scalar(dst[:, j, :], src[:, j, :], mv[:, j, 0:1], rstd[:, j:j + 1],
                                      ALU.subtract, ALU.mult)
    return ins


def phase_norm_x(nc, x_v, ident_d, xnT_d):
    with ExitStack() as ctx:
        m = Mem(nc, ctx, "nx")
        X = [m.sb(f"X{u}", [P, J, D]) for u in range(2)]
        XN = [m.sb(f"XN{u}", [P, J, D]) for u in range(2)]
        XT = [m.sb(f"XT{u}", [P, CC, GT]) for u in range(2)]
        stats = m.sb("stats", [P, J, 6])
        mv = m.sb("mv", [P, J, 2])
        veps = m.sb("veps", [P, J])
        rstd = m.sb("rstd", [P, J])
        nhalf = m.sb("nhalf", [P, J])
        ident = m.sb("ident", [P, P])
        PT = [m.ps(f"PT{u}", [P, CC, GT]) for u in range(2)]
        loaded = [m.sem(f"loaded{u}") for u in range(2)]
        stored = [m.sem(f"stored{u}") for u in range(2)]
        const_ld, half_set, var_ready, rstd_ready, xn_ready = (m.sem(n) for n in (
            "const_ld", "half_set", "var_ready", "rstd_ready", "xn_ready"))
        turned, evac, dve_chain, pool_chain, dve_step, pool_step = (m.sem(n) for n in (
            "turned", "evac", "dve_chain", "pool_chain", "dve_step", "pool_step"))
        out_v = xnT_d.rearrange("c p (g t) -> g p c t", t=GT)
        block = ctx.enter_context(nc.Block())
        R = NG // 2

        @block.sync
        def _(sp):
            sp.dma_start(ident[:, :], ident_d).then_inc(const_ld, 16)

            def body(i):
                for u in range(2):
                    wait(sp, xn_ready, 2 * i + u - 1)
                    sp.dma_start(X[u][:, :, :], group(x_v, 2 * i + u)).then_inc(loaded[u], 16)
            peeled(sp, R, body)

        @block.vector
        def _(dve):
            ch = Chain(dve, dve_chain, 2, dve_step)

            def body(i):
                ch.start(i)
                for u in range(2):
                    g = 2 * i + u
                    wait(dve, loaded[u], 16 * i + 16)
                    ln_stats(nc, ch, X[u], stats, mv, var_ready)
                    wait(dve, rstd_ready, g + 1)
                    wait(dve, turned, g - 1)
                    ln_apply(nc, X[u], mv, rstd, XN[u]).then_inc(xn_ready, 1)
            peeled(dve, R, body)

        @block.gpsimd
        def _(pool):
            ch = Chain(pool, pool_chain, 2, pool_step)
            nc.gpsimd.memset(nhalf[:, :], -0.5).then_inc(half_set, 1)
            pool.wait_ge(half_set, 1)

            def body(i):
                ch.start(i)
                for u in range(2):
                    g = 2 * i + u
                    wait(pool, xn_ready, g)
                    wait(pool, var_ready, g + 1, pool_step)
                    ln_rstd(nc, ch, mv, veps, rstd, nhalf, rstd_ready)
            peeled(pool, R, body)

        @block.tensor
        def _(pe):
            pe.wait_ge(const_ld, 16)

            def body(i):
                for u in range(2):
                    g = 2 * i + u
                    wait(pe, xn_ready, g + 1)
                    wait(pe, evac, g - 1)
                    for c in range(CC):
                        for j in range(J):
                            ins = nc.tensor.transpose(PT[u][:, c, j * P:(j + 1) * P],
                                                      XN[u][:, j, c * P:(c + 1) * P], ident[:, :])
                    ins.then_inc(turned, 1)
            peeled(pe, R, body)

        @block.scalar
        def _(act):
            def body(i):
                for u in range(2):
                    g = 2 * i + u
                    wait(act, turned, g + 1)
                    wait(act, stored[u], 16 * i)
                    nc.scalar.activation(XT[u][:, :, :], PT[u][:, :, :], ACT.Copy).then_inc(evac, 1)
                    wait(act, evac, g + 1)
                    act.dma_start(group(out_v, g), XT[u][:, :, :]).then_inc(stored[u], 16)
            peeled(act, R, body)
            for u in range(2):
                act.wait_ge(stored[u], 16 * R)

def phase_attention(nc, tag, H, DH, qkv_d, out_d, ident_d, sel_d):
    N = B * H
    NBLK = T // P
    NS = 3 * DH
    ROW_M = 96
    assert NS <= ROW_M and N % 4 == 0
    W = 512
    NCH = T // W
    STEPS = NCH * NBLK // 2
    SPC = NBLK // 2
    VW = 32 if DH + 1 <= 32 else 64
    NGRP = P // VW
    NMX = NBLK * T // 512
    MX_FROM = 18
    MX_EARLY = NMX * (STEPS - MX_FROM) // STEPS
    TURN_AT = 20
    TR_AT = (2, 4, 6, 8, 10, 12, 14, 16)
    FO_LAG = 3
    UNR = 4
    NPB = 8

    def spread(first, last, steps):
        n = last - first
        return [range(first + n * t // steps, first + n * (t + 1) // steps) for t in range(steps)]

    mx_of = [(1, x) for x in spread(MX_EARLY, NMX, MX_FROM)] + \
            [(2, x) for x in spread(0, MX_EARLY, STEPS - MX_FROM)]

    with ExitStack() as ctx:
        m = Mem(nc, ctx, tag)
        QKV = [m.sb(f"QKV{u}", [P, 3, NBLK, DH]) for u in range(2)]
        QS = m.sb("QS", [P, NBLK, NS], F32R)
        KS = m.sb("KS", [P, NBLK, NS], F32R)
        VS = [m.sb(f"VS{u}", [P, NBLK, VW]) for u in range(UNR)]
        QT = [m.sb(f"QT{u}", [P, T], F32R) for u in range(UNR)]
        KT = [m.sb(f"KT{u}", [P, T], F32R) for u in range(UNR)]
        PB = [m.sb(f"PB{u}", [P, 2, W]) for u in range(NPB)]
        AVS = [m.sb(f"AVS{u}", [P, W]) for u in range(2)]
        O = [m.sb(f"O{u}", [P, NBLK, DH]) for u in range(2)]
        NM4 = m.sb("NM4", [P, NBLK, T // 512])
        NM = m.sb("NM", [P, NBLK])
        NMF = m.sb("NMF", [NBLK, P])
        NMR = m.sb("NMR", [NBLK, 2, P], F32R)
        REC = m.sb("REC", [P, W // P])
        ident = m.sb("ident", [P, P])
        SEL = m.sb("SEL", [P, DH + 1])
        SP_ = [m.ps(f"S{u}", [P, 2, W]) for u in range(2)]
        MX = [m.ps(f"MX{u}", [P, 512]) for u in range(2)]
        AV = m.ps("AV", [P, W])
        MISC = m.ps("MISC", [P, 512])
        FO = MISC[:, 0:(W // P) * VW].rearrange("p (a b) -> p a b", b=VW)

        const_ld, preset, split_done, split_chain, part_chain, tr_put, tr_got = (m.sem(n) for n in (
            "const_ld", "preset", "split_done", "split_chain", "part_chain", "tr_put", "tr_got"))
        mx_put, mx_got, nm4_done, nm_ready, nmt_put, nmt_got = (m.sem(n) for n in (
            "mx_put", "mx_got", "nm4_done", "nm_ready", "nmt_put", "nmt_got"))
        nmr_ready, mrow, s_put, exp_done, av_done, avs_ready = (m.sem(n) for n in (
            "nmr_ready", "mrow", "s_put", "exp_done", "av_done", "avs_ready"))
        fo_put, rec_done, fo_got, pe_step, pool_step = (m.sem(n) for n in (
            "fo_put", "rec_done", "fo_got", "pe_step", "pool_step"))
        loaded = [m.sem(f"loaded{u}") for u in range(2)]
        ostored = [m.sem(f"ostored{u}") for u in range(2)]
        block = ctx.enter_context(nc.Block())

        def rounds(eng, window):
            for n in range(UNR):
                window(n, n)
            with eng.Fori(1, N // UNR - 1) as r:
                for s in range(UNR):
                    window(UNR * r + s, s)
            for n in range(N - UNR, N):
                window(n, n)

        def later(n, d):
            return not isinstance(n, int) or n + d < N

        @block.sync
        def _(sp):
            sp.dma_start(ident[:, :], ident_d).then_inc(const_ld, 16)
            sp.dma_start(SEL[:, :], sel_d).then_inc(const_ld, 16)

            def load(it, s):
                wait(sp, split_done, it - 1)
                sp.dma_start(QKV[s % 2][:, :, :, :], group(qkv_d, it)).then_inc(loaded[s % 2], 16)

            def m_row(it, s):
                wait(sp, nmr_ready, it + 1)
                for a in range(2):
                    sp.dma_start(QT[s % UNR][ROW_M + a:ROW_M + a + 1, :].bitcast(F32),
                                 NMR[:, a, :].bitcast(F32)).then_inc(mrow, 16)

            def store(it, s):
                wait(sp, fo_got, NCH * (it + 1))
                sp.dma_start(group(out_d, it), O[s % 2][:, :, :]).then_inc(ostored[s % 2], 16)

            for it in range(4):
                load(it, it)
            m_row(0, 0)

            def window(n, s):
                if later(n, 4):
                    load(n + 4, s + 4)
                if not isinstance(n, int) or n > 0:
                    store(n - 1, s + 3)
                if later(n, 1):
                    m_row(n + 1, s + 1)
            rounds(sp, window)
            store(N - 1, N - 1)
            for u in range(2):
                sp.wait_ge(ostored[u], 16 * (N // 2))

        @block.gpsimd
        def _(pool):
            for u in range(UNR):
                nc.gpsimd.memset(VS[u][:, :, :], 0.0).then_inc(preset, 1)
            for u in range(UNR):
                nc.gpsimd.memset(KT[u][:, :].bitcast(F32), 0.0).then_inc(preset, 1)
            pool.wait_ge(preset, 3 * UNR)
            for u in range(UNR):
                nc.gpsimd.memset(VS[u][:, :, DH:DH + 1], 1.0).then_inc(preset, 1)
            pool.wait_ge(preset, 4 * UNR)
            for u in range(UNR):
                nc.gpsimd.memset(KT[u][ROW_M:ROW_M + 2, :].bitcast(F32), 1.0).then_inc(preset, 1)

            def split(it, s):
                q, k, v = (QKV[s % 2][:, a, :, :] for a in range(3))
                qs = QS[:, :, :].rearrange("p b (a d) -> p b a d", a=3)
                ks = KS[:, :, :].rearrange("p b (a d) -> p b a d", a=3)
                wait(pool, nmr_ready, it - 2)
                wait(pool, tr_put, 8 * it)
                wait(pool, loaded[s % 2], 8 * it + 16 - 8 * (s % 2), pool_step)
                nc.gpsimd.tensor_copy(qs[:, :, 0, :], q)
                nc.gpsimd.tensor_copy(qs[:, :, 1, :], q)
                nc.gpsimd.tensor_copy(ks[:, :, 0, :], k)
                nc.gpsimd.tensor_copy(ks[:, :, 2, :], k)
                nc.gpsimd.tensor_copy(VS[s % UNR][:, :, 0:DH], v).then_inc(split_chain, 1)
                wait(pool, split_chain, it + 1)
                nc.gpsimd.tensor_tensor(qs[:, :, 2, :], q, qs[:, :, 0, :].bitcast(F32), ALU.subtract)
                nc.gpsimd.tensor_tensor(ks[:, :, 1, :], k, ks[:, :, 0, :].bitcast(F32),
                                        ALU.subtract).then_inc(split_done, 1)

            def m_parts(it, s):
                wait(pool, split_done, min(it + 3, N) if isinstance(it, int) else it + 3)
                wait(pool, mrow, 32 * it)
                wait(pool, nmt_got, it + 1, pool_step)
                nc.gpsimd.tensor_copy(NMR[:, 0, :], NMF[:, :]).then_inc(part_chain, 1)
                wait(pool, part_chain, it + 1)
                nc.gpsimd.tensor_tensor(NMR[:, 1, :], NMF[:, :], NMR[:, 0, :].bitcast(F32),
                                        ALU.subtract).then_inc(nmr_ready, 1)

            pool.wait_ge(preset, 5 * UNR)
            for it in range(3):
                split(it, it)
            m_parts(0, 0)

            def window(n, s):
                if later(n, 3):
                    split(n + 3, s + 3)
                if later(n, 1):
                    m_parts(n + 1, s + 1)
            rounds(pool, window)

        @block.tensor
        def _(pe):
            pe.wait_ge(const_ld, 32)
            pe.wait_ge(preset, 5 * UNR)

            def transposes(it, s, u, free):
                src = (KS if u < 4 else QS)
                if u == 0:
                    wait(pe, split_done, it + 1)
                wait(pe, *free, pe_step)
                for j in range(4):
                    ins = nc.tensor.transpose(MISC[0:NS, j * P:(j + 1) * P],
                                              src[:, 4 * (u % 4) + j, :].bitcast(F32), ident[:, :])
                ins.then_inc(tr_put, 1)
                return tr_got, 8 * it + u + 1

            def max_scores(it, s, x):
                if x == 0:
                    wait(pe, tr_got, 8 * it + 8)
                wait(pe, mx_got, NMX * it + x - 1)
                b, c = divmod(x, T // 512)
                nc.tensor.matmul(MX[x % 2][:, :], QT[s % UNR][0:ROW_M, b * P:(b + 1) * P],
                                 KT[s % UNR][0:ROW_M, c * 512:(c + 1) * 512],
                                 start=True, stop=True).then_inc(mx_put, 1)

            def max_turn(it, free):
                wait(pe, nm_ready, it + 1)
                wait(pe, *free)
                nc.tensor.transpose(MISC[0:NBLK, 0:P], NM[:, :], ident[:, :]).then_inc(nmt_put, 1)
                return nmt_got, it + 1

            def scores(it, s, t):
                c, kp = divmod(t, SPC)
                if t == 0:
                    wait(pe, mrow, 32 * it + 32)
                wait(pe, exp_done, STEPS * it + t - 1)
                for a in range(2):
                    kb = 2 * kp + a
                    ins = nc.tensor.matmul(SP_[t % 2][:, a, :], KT[s % UNR][0:ROW_M + 2, kb * P:(kb + 1) * P],
                                           QT[s % UNR][0:ROW_M + 2, c * W:(c + 1) * W],
                                           start=True, stop=True)
                ins.then_inc(s_put, 1)

            def values(it, s, v):
                c, vp = divmod(v, SPC // 2)
                if vp == 0:
                    wait(pe, avs_ready, NCH * it + c)
                wait(pe, exp_done, STEPS * it + 2 * v + 2)
                for a in range(4):
                    kb = 4 * vp + a
                    g = kb % NGRP
                    ins = nc.tensor.matmul(AV[g * VW:(g + 1) * VW, :], VS[s % UNR][:, kb, :],
                                           PB[(2 * v + a // 2) % NPB][:, a % 2, :],
                                           start=(kb < NGRP), stop=(kb >= NBLK - NGRP))
                ins.then_inc(av_done, 1)

            def regroup(it, c, free):
                wait(pe, avs_ready, NCH * it + c + 1)
                wait(pe, *free)
                for j in range(W // P):
                    ins = nc.tensor.matmul(FO[:, j, 0:DH + 1], AVS[c % 2][:, j * P:(j + 1) * P], SEL[:, :],
                                           start=True, stop=True)
                ins.then_inc(fo_put, 1)
                return fo_got, NCH * it + c + 1

            free = (tr_got, 0)
            for u in range(8):
                free = transposes(0, 0, u, free)
            for u in range(8):
                free = transposes(1, 1, u, free)
            for x in range(NMX):
                max_scores(0, 0, x)
            max_turn(0, free)
            for x in range(MX_EARLY):
                max_scores(1, 1, x)

            def window(n, s):
                free = (fo_got, NCH * n - 1) if not isinstance(n, int) or n > 0 else (nmt_got, 1)
                for t in range(STEPS):
                    ahead, tiles = mx_of[t]
                    if later(n, ahead):
                        for x in tiles[:1]:
                            max_scores(n + ahead, s + ahead, x)
                    scores(n, s, t)
                    if later(n, ahead):
                        for x in tiles[1:]:
                            max_scores(n + ahead, s + ahead, x)
                    if t % 2 and t >= 3:
                        values(n, s, t // 2 - 1)
                    elif t == 1 and (not isinstance(n, int) or n > 0):
                        values(n - 1, s + 3, STEPS // 2 - 1)
                    if t % SPC == FO_LAG:
                        c = t // SPC - 1
                        if c >= 0:
                            free = regroup(n, c, free)
                        elif not isinstance(n, int) or n > 0:
                            free = regroup(n - 1, NCH - 1, free)
                    if t in TR_AT and later(n, 2):
                        free = transposes(n + 2, s + 2, TR_AT.index(t), free)
                    if t == TURN_AT and later(n, 1):
                        free = max_turn(n + 1, free)
            rounds(pe, window)
            values(N - 1, N - 1, STEPS // 2 - 1)
            regroup(N - 1, NCH - 1, (fo_got, NCH * N - 1))

        @block.scalar
        def _(act):
            def put_transposed(it, s, u):
                dst = (KT if u < 4 else QT)[s % UNR]
                wait(act, tr_put, 8 * it + u + 1)
                if isinstance(it, int) and it == 0 and u == 0:
                    act.wait_ge(preset, 5 * UNR)
                nc.scalar.activation(dst[0:NS, (u % 4) * 4 * P:(u % 4 + 1) * 4 * P], MISC[0:NS, :],
                                     ACT.Copy).then_inc(tr_got, 1)

            def put_max(it):
                wait(act, nmt_put, it + 1)
                wait(act, nmr_ready, it)
                nc.scalar.activation(NMF[:, :], MISC[0:NBLK, 0:P], ACT.Copy).then_inc(nmt_got, 1)

            def exps(it, s, t):
                if t % 2 == 0:
                    wait(act, av_done, STEPS // 2 * it + (t - NPB) // 2 + 1)
                wait(act, s_put, STEPS * it + t + 1)
                nc.scalar.activation(PB[t % NPB][:, :, :], SP_[t % 2][:, :, :],
                                     ACT.Exp).then_inc(exp_done, 1)

            def put_sums(it, c):
                wait(act, fo_put, NCH * it + c - 1)
                wait(act, av_done, STEPS // 2 * it + SPC // 2 * (c + 1))
                nc.scalar.activation(AVS[c % 2][:, :], AV[:, :], ACT.Copy).then_inc(avs_ready, 1)

            for it in range(2):
                for u in range(8):
                    put_transposed(it, it, u)
            put_max(0)

            def window(n, s):
                for t in range(STEPS):
                    exps(n, s, t)
                    if t % SPC == 1:
                        if t > SPC:
                            put_sums(n, t // SPC - 1)
                        elif not isinstance(n, int) or n > 0:
                            put_sums(n - 1, NCH - 1)
                    if t in TR_AT and later(n, 2):
                        put_transposed(n + 2, s + 2, TR_AT.index(t))
                    if t == TURN_AT and later(n, 1):
                        put_max(n + 1)
            rounds(act, window)
            put_sums(N - 1, NCH - 1)

        @block.vector
        def _(dve):
            def maxima(it, x):
                b, c = divmod(x, T // 512)
                if x == 0:
                    wait(dve, nm_ready, it)
                wait(dve, mx_put, NMX * it + x + 1)
                nc.vector.tensor_reduce(NM4[:, b, c:c + 1], MX[x % 2][:, :], AX_X, ALU.max,
                                        negate=True).then_inc(mx_got, 1)
                if x == NMX - 1:
                    wait(dve, mx_got, NMX * it + NMX)
                    wait(dve, nmt_put, it)
                    nc.vector.tensor_reduce(NM[:, :], NM4[:, :, :], AX_X, ALU.min).then_inc(nm_ready, 1)

            def normalise(it, s, c):
                wait(dve, fo_put, NCH * it + c + 1)
                wait(dve, fo_got, NCH * it + c)
                nc.vector.reciprocal(REC[:, :], FO[:, :, DH]).then_inc(rec_done, 1)
                wait(dve, rec_done, NCH * it + c + 1)
                if c == 0:
                    wait(dve, ostored[s % 2], 8 * it - 8 * (s % 2))
                nc.vector.tensor_tensor(O[s % 2][:, 4 * c:4 * c + 4, :], FO[:, :, 0:DH],
                                        REC[:, :].to_broadcast([P, W // P, DH]), ALU.mult).then_inc(fo_got, 1)

            for u in range(UNR):
                nc.vector.memset(QT[u][:, :].bitcast(F32), 0.0).then_inc(preset, 1)
            for x in range(NMX):
                maxima(0, x)
            for x in range(MX_EARLY):
                maxima(1, x)

            def window(n, s):
                for t in range(STEPS):
                    ahead, tiles = mx_of[t]
                    if later(n, ahead):
                        for x in tiles:
                            maxima(n + ahead, x)
                    if t % SPC == FO_LAG:
                        c = t // SPC - 1
                        if c >= 0:
                            normalise(n, s, c)
                        elif not isinstance(n, int) or n > 0:
                            normalise(n - 1, s + 3, NCH - 1)
            rounds(dve, window)
            normalise(N - 1, N - 1, NCH - 1)

def phase_wkv(nc, xnT_d, wT_d, decay_d, first_d, ycat_d):
    TC = 1024
    UNITS = [(dr, h, c) for dr in range(2) for h in range(CC) for c in range(T // TC)]
    NU = len(UNITS)
    with ExitStack() as ctx:
        m = Mem(nc, ctx, "wkv")
        WT = m.sb("WT", [P, CC, 6 * D])
        XT = m.sb("XT", [P, CC, T])
        K, V, R = ([m.sb(f"{q}{u}", [P, TC]) for u in range(4)] for q in "KVR")
        MN, NUM, DEN = ([m.sb(f"{q}{u}", [P, TC + 1]) for u in range(2)] for q in ("MN", "NUM", "DEN"))
        E1S, E2S, E1, E2, EV, T2, Y = ([m.sb(f"{q}{u}", [P, TC]) for u in range(2)]
                                       for q in ("E1S", "E2S", "E1", "E2", "EV", "T2", "Y"))
        T1 = m.sb("T1", [P, TC])
        T3 = m.sb("T3", [P, TC])
        decay = m.sb("decay", [P, 2 * CC])
        w = m.sb("w", [P, 2 * CC])
        u_ = m.sb("u", [P, 2 * CC])
        PQ = [m.ps(f"PQ{q}", [P, TC]) for q in range(3)]
        const_ld, x_ld, w_exp, w_ready, proj, evac, mscan, dd = (m.sem(n) for n in (
            "const_ld", "x_ld", "w_exp", "w_ready", "proj", "evac", "mscan", "dd"))
        pd, relu, ex, pv, beta, chain, stored0, stored1, step = (m.sem(n) for n in (
            "pd", "relu", "ex", "pv", "beta", "chain", "stored0", "stored1", "step"))
        stored = [stored0, stored1]
        mrec = m.sem("recip")
        x_v = xnT_d.rearrange("c p (b t) -> b p c t", t=T)
        y_v = ycat_d.rearrange("q p (b t) -> b q p t", t=T)
        block = ctx.enter_context(nc.Block())
        ROW = {0: 1, 1: 2, 2: 0}

        def span(dr, c):
            return c * TC if dr == 0 else T - (c + 1) * TC

        def timed(ap, dr):
            return ap if dr == 0 else ap[:, ::-1]

        @block.sync
        def _(sp):
            sp.dma_start(WT[:, :, :], wT_d.rearrange("(c p) m -> p c m", p=P)).then_inc(const_ld, 16)
            sp.dma_start(decay[:, :], decay_d).then_inc(const_ld, 16)
            sp.dma_start(u_[:, :], first_d).then_inc(const_ld, 16)

            def store(b, n):
                dr, h, c = UNITS[n]
                yb = group(y_v, b)
                wait(sp, beta, NU * b + n + 1)
                sp.dma_start(yb[dr * CC + h, :, span(dr, c):span(dr, c) + TC],
                             Y[n % 2][:, :]).then_inc(stored[n % 2], 16)

            def body(b):
                wait(sp, proj, 3 * NU * b)
                sp.dma_start(XT[:, :, :], group(x_v, b)).then_inc(x_ld, 16)
                if not isinstance(b, int) or b > 0:
                    store(b - 1, NU - 1)
                for n in range(NU - 1):
                    store(b, n)
            peeled(sp, B, body)
            store(B - 1, NU - 1)
            for s in stored:
                sp.wait_ge(s, 16 * B * NU // 2)

        @block.tensor
        def _(pe):
            pe.wait_ge(const_ld, 48)

            def body(b):
                wait(pe, x_ld, 16 * b + 16)
                for n, (dr, h, c) in enumerate(UNITS):
                    g = NU * b + n
                    for q in range(3):
                        row = (dr * 3 + ROW[q]) * D + h * P
                        wait(pe, evac, 3 * g + q - 2)
                        for tt in range(TC // 512):
                            t0 = span(dr, c) + tt * 512
                            for cc in range(CC):
                                ins = nc.tensor.matmul(PQ[q][:, tt * 512:(tt + 1) * 512],
                                                       WT[:, cc, row:row + P], XT[:, cc, t0:t0 + 512],
                                                       start=(cc == 0), stop=(cc == CC - 1))
                        ins.then_inc(proj, 1)
            peeled(pe, B, body)

        @block.scalar
        def _(act):
            act.wait_ge(const_ld, 48)
            nc.scalar.activation(w[:, :], decay[:, :], ACT.Exp).then_inc(w_exp, 1)
            act.wait_ge(w_ready, 1)

            def body(b):
                for n, (dr, h, c) in enumerate(UNITS):
                    g = NU * b + n
                    s = n % 2
                    wait(act, beta, g - 3)
                    for q, (dst, f) in enumerate(((K, ACT.Copy), (V, ACT.Copy), (R, ACT.Sigmoid))):
                        wait(act, proj, 3 * g + q + 1)
                        nc.scalar.activation(timed(dst[n % 4][:, :], dr), PQ[q][:, :], f).then_inc(evac, 1)
                    j = dr * CC + h
                    wait(act, dd, g + 1)
                    wait(act, pd, 3 * g + 3)
                    nc.scalar.activation(E1S[s][:, :], E1S[s][:, :], ACT.Exp, bias=w[:, j:j + 1]).then_inc(ex, 1)
                    nc.scalar.activation(E2S[s][:, :], E2S[s][:, :], ACT.Exp).then_inc(ex, 1)
                    nc.scalar.activation(E1[s][:, :], E1[s][:, :], ACT.Relu).then_inc(relu, 1)
                    nc.scalar.activation(E2[s][:, :], E2[s][:, :], ACT.Exp).then_inc(ex, 1)
                    wait(act, relu, g + 1)
                    nc.scalar.activation(E1[s][:, :], E1[s][:, :], ACT.Exp, scale=-1.0).then_inc(ex, 1)
            peeled(act, B, body)

        @block.gpsimd
        def _(pool):
            def body(b):
                for n, (dr, h, c) in enumerate(UNITS):
                    g = NU * b + n
                    s = n % 2
                    wait(pool, beta, g - 1)
                    wait(pool, mscan, g + 1)
                    nc.gpsimd.tensor_tensor(E1S[s][:, :], MN[s][:, 0:TC], MN[s][:, 1:TC + 1],
                                            ALU.subtract).then_inc(pd, 1)
                    nc.gpsimd.tensor_tensor(E2S[s][:, :], K[n % 4][:, :], MN[s][:, 1:TC + 1],
                                            ALU.subtract).then_inc(pd, 1)
                    wait(pool, dd, g + 1, step)
                    nc.gpsimd.tensor_scalar(E2[s][:, :], E1[s][:, :], 0.0, None, ALU.min).then_inc(pd, 1)
                    wait(pool, ex, 4 * g + 2)
                    nc.gpsimd.tensor_tensor(EV[s][:, :], E2S[s][:, :], V[n % 4][:, :],
                                            ALU.mult).then_inc(pv, 1)
                    wait(pool, ex, 4 * g + 3)
                    nc.gpsimd.tensor_tensor(T2[s][:, :], E2[s][:, :], V[n % 4][:, :],
                                            ALU.mult).then_inc(pv, 1)
            peeled(pool, B, body)

        @block.vector
        def _(dve):
            dve.wait_ge(w_exp, 1)
            nc.vector.tensor_scalar(w[:, :], w[:, :], -1.0, None, ALU.mult).then_inc(w_ready, 1)
            dve.wait_ge(w_ready, 1)
            LINKS = 10

            def alpha(b, n):
                dr, h, c = UNITS[n]
                j, s, g = dr * CC + h, n % 2, NU * b + n
                base = 0 if isinstance(b, int) and g == 0 else LINKS * g - 9
                if c == 0:
                    nc.vector.memset(MN[s][:, 0:1], -1e38).then_inc(chain, 1)
                else:
                    nc.vector.tensor_copy(MN[s][:, 0:1], MN[1 - s][:, TC:TC + 1]).then_inc(chain, 1)
                wait(dve, evac, 3 * g + 1)
                wait(dve, chain, base + 1)
                nc.vector.tensor_tensor_scan(MN[s][:, 1:TC + 1], w[:, j:j + 1].to_broadcast([P, TC]),
                                             K[n % 4][:, :], MN[s][:, 0:1], ALU.add, ALU.max).then_inc(mscan, 1)
                wait(dve, mscan, g + 1)
                nc.vector.scalar_tensor_tensor(out=E1[s][:, :], in0=K[n % 4][:, :], scalar=u_[:, j:j + 1],
                                               in1=MN[s][:, 0:TC], op0=ALU.add, op1=ALU.subtract).then_inc(dd, 1)

            def outputs(b, n):
                dr, h, c = UNITS[n]
                s, g = n % 2, NU * b + n
                base = LINKS * g + 2 if not (isinstance(b, int) and g == NU * B - 1) else LINKS * g + 1
                if c == 0:
                    nc.vector.memset(NUM[s][:, 0:1], 0.0).then_inc(chain, 1)
                    nc.vector.memset(DEN[s][:, 0:1], 0.0).then_inc(chain, 1)
                else:
                    nc.vector.tensor_copy(NUM[s][:, 0:1], NUM[1 - s][:, TC:TC + 1]).then_inc(chain, 1)
                    nc.vector.tensor_copy(DEN[s][:, 0:1], DEN[1 - s][:, TC:TC + 1]).then_inc(chain, 1)
                wait(dve, chain, base + 2)
                wait(dve, pv, 2 * g + 1)
                nc.vector.tensor_tensor_scan(NUM[s][:, 1:TC + 1], E1S[s][:, :], EV[s][:, :], NUM[s][:, 0:1],
                                             ALU.mult, ALU.add).then_inc(chain, 1)
                nc.vector.tensor_tensor_scan(DEN[s][:, 1:TC + 1], E1S[s][:, :], E2S[s][:, :], DEN[s][:, 0:1],
                                             ALU.mult, ALU.add).then_inc(chain, 1)
                wait(dve, ex, 4 * g + 4)
                wait(dve, chain, base + 3)
                nc.vector.tensor_tensor(T1[:, :], E1[s][:, :], NUM[s][:, 0:TC], ALU.mult).then_inc(chain, 1)
                wait(dve, chain, base + 4)
                nc.vector.tensor_tensor(T3[:, :], E1[s][:, :], DEN[s][:, 0:TC], ALU.mult).then_inc(chain, 1)
                wait(dve, pv, 2 * g + 2)
                wait(dve, chain, base + 5)
                nc.vector.tensor_tensor(T1[:, :], T1[:, :], T2[s][:, :], ALU.add).then_inc(chain, 1)
                wait(dve, chain, base + 6)
                nc.vector.tensor_tensor(T3[:, :], T3[:, :], E2[s][:, :], ALU.add).then_inc(chain, 1)
                wait(dve, chain, base + 7)
                wait(dve, evac, 3 * g + 3)
                nc.vector.tensor_tensor(T1[:, :], T1[:, :], R[n % 4][:, :], ALU.mult).then_inc(chain, 1)
                wait(dve, chain, base + 8)
                nc.vector.reciprocal(T3[:, :], T3[:, :]).then_inc(mrec, 1)
                wait(dve, mrec, g + 1)
                wait(dve, chain, base + 9)
                wait(dve, stored[s], 8 * NU * b + 16 * (n // 2))
                nc.vector.tensor_tensor(timed(Y[s][:, :], dr), T1[:, :], T3[:, :], ALU.mult).then_inc(beta, 1)

            def body(b):
                for n in range(NU):
                    alpha(b, n)
                    if n > 0:
                        outputs(b, n - 1)
                    elif not isinstance(b, int) or b > 0:
                        outputs(b - 1, NU - 1)
            peeled(dve, B, body)
            outputs(B - 1, NU - 1)

EXPERTS = 32
HEADS1, DH1 = 16, 16
HEADS2, DH2 = 8, 32


def phase_rows(nc, tag, src_kind, src, x_d, xnew_d, ident_d, post_kind, post, xn_d=None):
    E4 = T // GT
    NL = 3 if post_kind == "sliced" else 2
    H, DH = (HEADS1, DH1) if post_kind == "rope" else (HEADS2, DH2)
    with ExitStack() as ctx:
        m = Mem(nc, ctx, tag)
        X = [m.sb(f"X{u}", [P, J, D]) for u in range(2)]
        XN = [m.sb(f"XN{u}", [P, J, D]) for u in range(2)]
        TMP = m.sb("TMP", [P, J, D])
        XT = [m.sb(f"XT{u}", [P, CC, GT]) for u in range(2)]
        stats, mv, veps, rstd = ([m.sb(f"{q}{k}", [P, J] + e) for k in range(NL)]
                                 for q, e in (("stats", [6]), ("mv", [2]), ("veps", []), ("rstd", [])))
        nhalf = m.sb("nhalf", [P, J])
        ident = m.sb("ident", [P, P])
        PT = m.ps("PT", [P, CC, GT])
        if src_kind != "heads":
            PA = m.ps("PA", [P, J, D])
        if src_kind == "scan":
            A = [m.sb(f"A{u}", [P, 2 * CC, GT]) for u in range(2)]
            OW = m.sb("OW", [P, 2 * CC, D])
        elif src_kind == "experts":
            A = [m.sb(f"A{u}", [EXPERTS, GT]) for u in range(2)]
            A2 = [m.sb(f"A2{u}", [EXPERTS, D]) for u in range(2)]
        else:
            A = [m.sb(f"A{u}", [P, HEADS1, J, DH1]) for u in range(2)]
        if post_kind == "gate":
            GW = m.sb("GW", [P, CC, EXPERTS])
            GB = m.sb("GB", [EXPERTS, 1])
            LG = [m.sb(f"LG{u}", [EXPERTS, GT]) for u in range(2)]
            PG = m.ps("PG", [EXPERTS, GT])
            TILES = 1
        else:
            WQ = m.sb("WQ", [P, CC, 3 * D])
            QB = m.sb("QB", [P, H, 3, T // P, DH])
            PO = [m.ps(f"PO{u}", [P, 2, 512]) for u in range(2)]
            TILES = J
        if post_kind == "rope":
            ROPE = m.sb("ROPE", [P, T // P, 2, 2, DH // 2])
            RT = [m.sb(f"RT{k}", [P, 2, H, DH // 2]) for k in range(4)]
        if post_kind == "sliced":
            XI = [m.sb(f"XI{u}", [P, J, D]) for u in range(2)]
            NW = m.sb("NW", [P, 2, D])
            BIAS = m.sb("BIAS", [P, 3, D])
        names = ("const_ld", "half_set", "bias_ready", "a_done", "var", "rs", "xnew", "xn", "xi", "turned", "xt",
                 "proj", "post_done", "v_done", "chain", "pool_chain", "ro", "stored_b", "step", "pstep", "sstep", "pe_step")
        (const_ld, half_set, bias_ready, a_done, var, rs, xnew, xn_ready, xi_ready, turned, xt,
         proj, post_done, v_done, chain, pool_chain, ro, stored_b, step, pstep, sstep, pe_step) = (m.sem(n) for n in names)
        a_ld, x_ld, x_st, n_st, l_st = ([m.sem(f"{n}{u}") for u in range(2)]
                                        for n in ("a_ld", "x_ld", "x_st", "n_st", "l_st"))
        inner = xi_ready if post_kind == "sliced" else xn_ready
        NCONST = 1 + {"scan": 1}.get(src_kind, 0) + {"gate": 2, "rope": 2, "sliced": 4}[post_kind]
        A_LOADS = 2 if src_kind == "experts" else 1
        SG = max(1, 512 // (J * DH * 4))
        block = ctx.enter_context(nc.Block())

        def a_tile(u, j):
            return PA[:, j, :] if src_kind != "heads" else A[u][:, :, j, :]

        def before(b, e):
            if e > 0:
                return b, e - 1
            return None if isinstance(b, int) and b == 0 else (b - 1, E4 - 1)

        def qb_free(b, e):
            return 48 * (E4 // SG) * b + 48 * (e // SG + 1 - E4 // SG)

        @block.sync
        def _(sp):
            def const(dst, ap):
                sp.dma_start(dst, ap).then_inc(const_ld, 16)
            const(ident[:, :], ident_d)
            if src_kind == "scan":
                const(OW[:, :, :], src[1].rearrange("(q p) n -> p q n", p=P))
            if post_kind == "gate":
                const(GW[:, :, :], post[0].rearrange("(c p) n -> p c n", p=P))
                const(GB[:, :], post[1])
            else:
                const(WQ[:, :, :], post[0].rearrange("(c p) n -> p c n", p=P))
            if post_kind == "rope":
                const(ROPE[:, :, :, :, :], post[1])
            if post_kind == "sliced":
                const(BIAS[:, :, :], post[1].partition_broadcast(P))
                const(NW[:, 0, :], post[2].partition_broadcast(P))
                const(NW[:, 1, :], post[3].partition_broadcast(P))

            def load(b, e):
                g, u = E4 * b + e, e % 2
                k = 16 * A_LOADS
                wait(sp, a_done if src_kind != "heads" else xnew, g - 1, sstep)
                if src_kind == "scan":
                    sp.dma_start(A[u][:, :, :], group(src[0].rearrange("q p (g t) -> g p q t", t=GT), g))\
                        .then_inc(a_ld[u], 16)
                elif src_kind == "experts":
                    wb = group(src[0], b)
                    sp.dma_start(A[u][:, :], wb[:, e * GT:(e + 1) * GT]).then_inc(a_ld[u], 16)
                    sp.dma_start(A2[u][:, :], group(src[1], b)).then_inc(a_ld[u], 16)
                else:
                    ab = group(src[0].rearrange("(b h) p n d -> b p h n d", b=B), b)
                    sp.dma_start(A[u][:, :, :, :], ab[:, :, e * J:(e + 1) * J, :]).then_inc(a_ld[u], 16)
                wait(sp, xn_ready, g - 1, sstep)
                wait(sp, x_st[u], 8 * E4 * b + 16 * (e // 2), sstep)
                sp.dma_start(X[u][:, :, :], group(tokens(x_d), g)).then_inc(x_ld[u], 16)

            def store(b, e):
                g, u = E4 * b + e, e % 2
                wait(sp, xnew, g + 1, sstep)
                sp.dma_start(group(tokens(xnew_d), g), X[u][:, :, :]).then_inc(x_st[u], 16)
                if xn_d is not None:
                    wait(sp, xn_ready, g + 1, sstep)
                    sp.dma_start(group(tokens(xn_d), g), XN[u][:, :, :]).then_inc(n_st[u], 16)

            def store_post(b, e):
                g, u = E4 * b + e, e % 2
                if post_kind == "gate":
                    wait(sp, post_done, g + 1, sstep)
                    lb = group(post[2], b)
                    sp.dma_start(lb[:, e * GT:(e + 1) * GT], LG[u][:, :]).then_inc(l_st[u], 16)
                elif (e + 1) % SG == 0:
                    wait(sp, post_done, TILES * (g + 1), sstep)
                    wait(sp, v_done, TILES * (g + 1), sstep)
                    blks = slice(J * (e + 1 - SG), J * (e + 1))
                    out = group(post[-1].rearrange("(b h) p a n d -> b p h a n d", b=B), b)
                    for a in range(3):
                        sp.dma_start(out[:, :, a, blks, :], QB[:, :, a, blks, :]).then_inc(stored_b, 16)

            def body(b):
                for e in range(E4):
                    load(b, e)
                    if before(b, e):
                        store(*before(b, e))
                        if e >= 2:
                            store_post(b, e - 2)
                        elif before(b, 0):
                            store_post(b - 1, E4 + e - 2)
            peeled(sp, B, body)
            store(B - 1, E4 - 1)
            store_post(B - 1, E4 - 2)
            store_post(B - 1, E4 - 1)
            for u in range(2):
                sp.wait_ge(x_st[u], 8 * B * E4)
                if xn_d is not None:
                    sp.wait_ge(n_st[u], 8 * B * E4)
                if post_kind == "gate":
                    sp.wait_ge(l_st[u], 8 * B * E4)
            if post_kind != "gate":
                sp.wait_ge(stored_b, 48 * B * E4 // SG)

        @block.gpsimd
        def _(pool):
            nc.gpsimd.memset(nhalf[:, :], -0.5).then_inc(half_set, 1)
            pool.wait_ge(half_set, 1)

            def body(b):
                for e in range(E4):
                    for k in range(NL):
                        r = NL * (E4 * b + e) + k
                        wait(pool, var, r + 1, pstep)
                        nc.gpsimd.tensor_scalar(veps[k][:, :], mv[k][:, :, 1], EPS, None,
                                                ALU.add).then_inc(pool_chain, 1)
                        wait(pool, pool_chain, r + 1)
                        nc.gpsimd.tensor_tensor(rstd[k][:, :], veps[k][:, :], nhalf[:, :],
                                                ALU.pow).then_inc(rs, 1)
            peeled(pool, B, body)

        @block.tensor
        def _(pe):
            pe.wait_ge(const_ld, 16 * NCONST)

            def source(b, e):
                if src_kind == "heads":
                    return
                g, u = E4 * b + e, e % 2
                wait(pe, a_ld[u], 8 * E4 * A_LOADS * b + 16 * A_LOADS * (e // 2 + 1))
                wait(pe, xnew, g, pe_step)
                for j in range(J):
                    t = slice(j * P, (j + 1) * P)
                    if src_kind == "scan":
                        for q in range(2 * CC):
                            ins = nc.tensor.matmul(PA[:, j, :], A[u][:, q, t], OW[:, q, :],
                                                   start=(q == 0), stop=(q == 2 * CC - 1))
                    else:
                        ins = nc.tensor.matmul(PA[:, j, :], A[u][:, t], A2[u][:, :], start=True, stop=True)
                ins.then_inc(a_done, 1)

            def turn(b, e):
                g, u = E4 * b + e, e % 2
                S = XI if post_kind == "sliced" else XN
                wait(pe, inner, g + 1)
                wait(pe, xt, g)
                for c in range(CC):
                    for j in range(J):
                        ins = nc.tensor.transpose(PT[:, c, j * P:(j + 1) * P],
                                                  S[u][:, j, c * P:(c + 1) * P], ident[:, :])
                ins.then_inc(turned, 1)

            def project(b, e):
                g, u = E4 * b + e, e % 2
                wait(pe, xt, g + 1)
                if post_kind == "gate":
                    wait(pe, post_done, g, pe_step)
                    for c in range(CC):
                        ins = nc.tensor.matmul(PG[:, :], GW[:, c, :], XT[u][:, c, :],
                                               start=(c == 0), stop=(c == CC - 1))
                    ins.then_inc(proj, 1)
                    return
                rows = D >> e if post_kind == "sliced" else D
                ks = [min(P, rows - c * P) for c in range(CC) if rows > c * P]
                for j in range(J):
                    wait(pe, post_done, TILES * g + j - 1, pe_step)
                    wait(pe, v_done, TILES * g + j - 1, pe_step)
                    for lo, n in ((0, 512), (512, 3 * D - 512)):
                        for c, k in enumerate(ks):
                            ins = nc.tensor.matmul(PO[j % 2][:, lo // 512, 0:n],
                                                   XT[u][0:k, c, j * P:(j + 1) * P], WQ[0:k, c, lo:lo + n],
                                                   start=(c == 0), stop=(c == len(ks) - 1))
                    ins.then_inc(proj, 1)

            def body(b):
                for e in range(E4):
                    if e == 0 and isinstance(b, int) and b == 0:
                        source(b, e)
                    if before(b, e):
                        project(*before(b, e))
                    if following(b, e, E4):
                        source(*following(b, e, E4))
                    turn(b, e)
            peeled(pe, B, body, last=True)
            project(B - 1, E4 - 1)

        @block.scalar
        def _(act):
            act.wait_ge(const_ld, 16 * NCONST)

            def copy_turned(b, e):
                g, u = E4 * b + e, e % 2
                wait(act, turned, g + 1)
                wait(act, proj, TILES * (g - 1))
                nc.scalar.activation(XT[u][:, :, :], PT[:, :, :], ACT.Copy).then_inc(xt, 1)

            def post_act(b, e):
                g, u = E4 * b + e, e % 2
                if post_kind == "gate":
                    wait(act, proj, g + 1)
                    wait(act, l_st[u], 8 * E4 * b + 16 * (e // 2))
                    nc.scalar.activation(LG[u][:, :], PG[:, :], ACT.Identity, bias=GB[:, 0:1])\
                        .then_inc(post_done, 1)
                    return
                wait(act, stored_b, qb_free(b, e))
                for j in range(J):
                    wait(act, proj, TILES * g + j + 1)
                    v = PO[j % 2][:, 1, 0:D].rearrange("p (h d) -> p h d", d=DH)
                    if post_kind == "rope":
                        nc.scalar.activation(QB[:, :, 2, J * e + j, :], v, ACT.Copy).then_inc(v_done, 1)

            def body(b):
                for e in range(E4):
                    if before(b, e):
                        post_act(*before(b, e))
                    copy_turned(b, e)
            peeled(act, B, body)
            post_act(B - 1, E4 - 1)

        @block.vector
        def _(dve):
            dve.wait_ge(const_ld, 16 * NCONST)
            ALINKS = NL + 1 + (2 if post_kind == "sliced" else 0)
            ch = Chain(dve, chain, ALINKS * E4, step)
            if post_kind == "sliced":
                nc.vector.tensor_scalar(BIAS[:, 0, :], BIAS[:, 0, :], D ** -0.5, None, ALU.mult).then_inc(bias_ready, 1)
                dve.wait_ge(bias_ready, 1)

            def ln(k, b, e, part, srcs, dst=None):
                r = NL * (E4 * b + e) + k
                if part == 0:
                    for j in range(J):
                        ins = nc.vector.bn_stats(stats[k][:, j, :], srcs[j])
                    ch.link(ins, apart=True)
                    for j in range(J):
                        ins = nc.vector.bn_aggr(mv[k][:, j, :], stats[k][:, j, :])
                    ins.then_inc(var, 1)
                    return
                wait(dve, rs, r + 1)
                for j in range(J):
                    ins = nc.vector.tensor_scalar(dst[:, j, :] if len(srcs[j].shape) == 2 else
                                                  dst[:, j, :].rearrange("p (h d) -> p h d", d=DH1),
                                                  srcs[j], mv[k][:, j, 0:1],
                                                  rstd[k][:, j:j + 1], ALU.subtract, ALU.mult)
                return ins

            def post_dve(b, e, js):
                g, u = E4 * b + e, e % 2
                for j in js:
                    wait(dve, proj, TILES * g + j + 1)
                    blk = J * e + j
                    if j == 0:
                        wait(dve, stored_b, qb_free(b, e))
                    if post_kind == "rope":
                        qk = PO[j % 2][:, 0, :].rearrange("p (a h i r) -> p a h i r", a=2, h=H, r=2)
                        cs = [ROPE[:, blk, f, :, :].unsqueeze(2).to_broadcast([P, 2, H, DH // 2])
                              for f in range(2)]
                        wait(dve, post_done, TILES * g + j)
                        for k, (r, f) in enumerate(((0, 0), (1, 1), (0, 1), (1, 0))):
                            ins = nc.vector.tensor_tensor(RT[k][:, :, :, :], qk[:, :, :, :, r],
                                                          cs[f][:, :, :, :], ALU.mult)
                        ins.then_inc(ro, 1)
                        wait(dve, ro, TILES * g + j + 1)
                        for a in range(2):
                            out = QB[:, :, a, blk, :].rearrange("p h (i r) -> p h i r", r=2)
                            nc.vector.tensor_tensor(out[:, :, :, 0], RT[0][:, a], RT[1][:, a], ALU.subtract)
                            ins = nc.vector.tensor_tensor(out[:, :, :, 1], RT[2][:, a], RT[3][:, a], ALU.add)
                        ins.then_inc(post_done, 1)
                    else:
                        view = [PO[j % 2][:, 0, 0:D], PO[j % 2][:, 0, D:2 * D], PO[j % 2][:, 1, 0:D]]
                        out = [QB[:, :, a, blk, :] for a in range(3)]
                        hd = [v.rearrange("p (h d) -> p h d", d=DH) for v in view]
                        bb = [BIAS[:, a, :].rearrange("p (h d) -> p h d", d=DH) for a in range(3)]
                        nc.vector.scalar_tensor_tensor(out=out[0], in0=hd[0], scalar=D ** -0.5, in1=bb[0],
                                                       op0=ALU.mult, op1=ALU.add)
                        nc.vector.tensor_tensor(out[1], hd[1], bb[1], ALU.add).then_inc(post_done, 1)
                        nc.vector.tensor_tensor(out[2], hd[2], bb[2], ALU.add).then_inc(v_done, 1)

            def body(b):
                ch.start(b)
                for e in range(E4):
                    g, u = E4 * b + e, e % 2
                    prev = before(b, e) if post_kind != "gate" else None
                    if src_kind == "heads":
                        wait(dve, a_ld[u], 8 * E4 * b + 16 * (e // 2 + 1))
                    else:
                        wait(dve, a_done, g + 1)
                    at = [a_tile(u, j) for j in range(J)]
                    xt_ = [X[u][:, j, :] for j in range(J)]
                    ln(0, b, e, 0, at)
                    ch.link(ln(0, b, e, 1, at, TMP))
                    wait(dve, x_ld[u], 8 * E4 * b + 16 * (e // 2 + 1))
                    nc.vector.tensor_tensor(X[u][:, :, :], X[u][:, :, :], TMP[:, :, :], ALU.add).then_inc(xnew, 1)
                    wait(dve, xnew, g + 1)
                    ln(1, b, e, 0, xt_)
                    if prev:
                        post_dve(*prev, range(0, J // 2))
                    if xn_d is not None:
                        wait(dve, n_st[u], 8 * E4 * b + 16 * (e // 2))
                    wait(dve, turned, g - 1)
                    ln(1, b, e, 1, xt_, XN[u]).then_inc(xn_ready, 1)
                    if prev and post_kind == "rope":
                        post_dve(*prev, range(J // 2, J))
                    if post_kind == "sliced":
                        wait(dve, xn_ready, g + 1)
                        nt = [XN[u][:, j, :] for j in range(J)]
                        ln(2, b, e, 0, nt)
                        if prev:
                            post_dve(*prev, range(J // 2, J))
                        ch.link(ln(2, b, e, 1, nt, XI[u]))
                        ch.link(nc.vector.tensor_tensor(XI[u][:, :, :], XI[u][:, :, :],
                                                        NW[:, 0:1, :].to_broadcast([P, J, D]), ALU.mult))
                        nc.vector.tensor_tensor(XI[u][:, :, :], XI[u][:, :, :],
                                                NW[:, 1:2, :].to_broadcast([P, J, D]), ALU.add).then_inc(xi_ready, 1)
                ch.end()
            peeled(dve, B, body)
            if post_kind != "gate":
                post_dve(B - 1, E4 - 1, range(J))

def phase_experts(nc, lg_d, xn_d, w1_d, w2_d, pick_d, ident_d, w_d, o_d):
    HID = 1024
    NB, HC = T // P, HID // P
    NE = EXPERTS
    EG = NE // 4
    BE = B * NE
    with ExitStack() as ctx:
        m = Mem(nc, ctx, "moe")
        LG = m.sb("LG", [BE, T])
        TOP = m.sb("TOP", [BE, 8])
        RP = m.sb("RP", [BE, T])
        nmax, total, rtotal = (m.sb(n, [BE, 1]) for n in ("nmax", "total", "rtotal"))
        WTS = m.sb("WTS", [P, NB, BE])
        XB = [m.sb(f"XB{u}", [P, NB, D]) for u in range(2)]
        MTS = m.sb("MTS", [P, CC, NE, B])
        ME = m.sb("ME", [P, CC, 4, B])
        PICK = m.sb("PICK", [NE, NE, B])
        PK = m.sb("PK", [NE, 4, B])
        W1 = [m.sb(f"W1{u}", [P, 4, CC, HID]) for u in range(2)]
        W2 = [m.sb(f"W2{u}", [P, 4, HC, D]) for u in range(2)]
        B1 = m.sb("B1", [NE, HID])
        B2 = m.sb("B2", [NE, D])
        HS = m.sb("HS", [P, HID])
        HT = m.sb("HT", [P, HC, 4, B])
        OS = m.sb("OS", [P, EG, D])
        ident = m.sb("ident", [P, P])
        PH = m.ps("PH", [P, HID])
        TP = m.ps("TP", [P, HC, P])
        PM = m.ps("PM", [P, 512])
        PO = m.ps("PO", [P, 512])
        names = ("const_ld", "lg_ld", "nmax_done", "zeroed", "exp_done", "soft", "w_done", "w_st", "wt_put",
                 "wt_got", "mts_done", "me_done", "h_put", "h_got", "t_put", "t_got", "o_put",
                 "o_got", "o_st", "xb_used", "sp_step", "dve_step", "pe_step", "act_step")
        (const_ld, lg_ld, nmax_done, zeroed, exp_done, soft, w_done, w_st, wt_put,
         wt_got, mts_done, me_done, h_put, h_got, t_put, t_got, o_put,
         o_got, o_st, xb_used, sp_step, dve_step, pe_step, act_step) = (m.sem(n) for n in names)
        w1_ld, w2_ld, x_ld = ([m.sem(f"{n}{u}") for u in range(2)] for n in ("w1_ld", "w2_ld", "x_ld"))
        xb_v = xn_d.rearrange("(b n p) d -> b p n d", b=B, p=P)
        w1_v = w1_d[:, 0:D, :].rearrange("(g k) (c p) n -> g p k c n", k=4, p=P)
        w2_v = w2_d[:, 0:HID, :].rearrange("(g k) (c p) n -> g p k c n", k=4, p=P)
        block = ctx.enter_context(nc.Block())

        def part(v, eg, k):
            if isinstance(eg, int):
                return v[eg][:, k]
            return v[bass.ds(eg, 1), :, k].rearrange("o p c n -> (o p) c n")

        @block.sync
        def _(sp):
            sp.dma_start(LG[:, :], lg_d.rearrange("b e t -> (b e) t")).then_inc(lg_ld, 16)
            for b in range(2):
                sp.dma_start(XB[b][:, :, :], xb_v[b]).then_inc(x_ld[b], 16)
            for dst, ap in ((ident[:, :], ident_d), (PICK[:, :, :], pick_d), (B1[:, :], w1_d[:, D, :]),
                            (B2[:, :], w2_d[:, HID, :])):
                sp.dma_start(dst, ap).then_inc(const_ld, 16)

            def load(eg, u):
                wait(sp, h_put, eg - 1, sp_step)
                for k in range(4):
                    sp.dma_start(W1[u][:, k, :, :], part(w1_v, eg, k)).then_inc(w1_ld[u], 16)
                wait(sp, o_put, eg - 1, sp_step)
                for k in range(4):
                    sp.dma_start(W2[u][:, k, :, :], part(w2_v, eg, k)).then_inc(w2_ld[u], 16)

            for eg in range(2):
                load(eg, eg)
            for b in range(2, B):
                sp.wait_ge(xb_used, b - 1)
                sp.dma_start(XB[b % 2][:, :, :], xb_v[b]).then_inc(x_ld[b % 2], 16)
            sp.wait_ge(w_done, 1)
            sp.dma_start(w_d.rearrange("b e t -> (b e) t"), LG[:, :]).then_inc(w_st, 16)
            with sp.Fori(1, EG // 2) as i:
                for u in range(2):
                    load(2 * i + u, u)
            sp.wait_ge(o_got, 4 * EG)
            for k in range(4):
                sp.dma_start(o_d.rearrange("b (g k) d -> k b g d", k=4)[k],
                             OS[32 * k:32 * k + B, :, :]).then_inc(o_st, 16)
            sp.wait_ge(w_st, 16)
            sp.wait_ge(o_st, 64)

        @block.vector
        def _(dve):
            nc.vector.memset(HS[:, :], 0.0).then_inc(zeroed, 1)
            dve.wait_ge(lg_ld, 16)
            nc.vector.tensor_reduce(nmax[:, :], LG[:, :], AX_X, ALU.max, negate=True).then_inc(nmax_done, 1)
            dve.wait_ge(exp_done, 1)
            nc.vector.reciprocal(rtotal[:, :], total[:, :]).then_inc(soft, 1)
            dve.wait_ge(soft, 1)
            nc.vector.tensor_scalar(LG[:, :], LG[:, :], rtotal[:, 0:1], None, ALU.mult).then_inc(soft, 1)
            dve.wait_ge(soft, 2)
            nc.vector.max(TOP[:, :], LG[:, :]).then_inc(soft, 1)
            dve.wait_ge(soft, 3)
            nc.vector.match_replace(RP[:, :], TOP[:, :], LG[:, :], 0.0).then_inc(soft, 1)
            dve.wait_ge(soft, 4)
            nc.vector.tensor_tensor(LG[:, :], LG[:, :], RP[:, :], ALU.subtract).then_inc(w_done, 1)
            for n in range(NB // HC):
                dve.wait_ge(wt_put, n + 1)
                nc.vector.tensor_copy(WTS[:, n * HC:(n + 1) * HC, :], TP[:, :, :]).then_inc(wt_got, 1)
            dve.wait_ge(xb_used, B)
            for c in range(CC):
                nc.vector.tensor_copy(MTS[:, c, :, :], PM[:, c * BE:(c + 1) * BE]
                                      .rearrange("p (b e) -> p e b", b=B)).then_inc(mts_done, 1)
            dve.wait_ge(mts_done, CC)
            dve.wait_ge(const_ld, 64)

            def round_(eg):
                wait(dve, o_put, eg, dve_step)
                if isinstance(eg, int):
                    a, b = MTS[:, :, 4 * eg:4 * eg + 4, :], PICK[:, 4 * eg:4 * eg + 4, :]
                else:
                    a, b = MTS[:, :, bass.ds(4 * eg, 4), :], PICK[:, bass.ds(4 * eg, 4), :]
                nc.vector.tensor_copy(ME[:, :, :, :], a).then_inc(me_done, 1)
                nc.vector.tensor_copy(PK[:, :, :], b).then_inc(me_done, 1)
                wait(dve, t_put, eg + 1, dve_step)
                nc.vector.tensor_copy(HT[:, :, :, :], TP[:, :, :].rearrange("p c (k x) -> p c k x", k=4)
                                      [:, :, :, 0:B]).then_inc(t_got, 1)
                wait(dve, o_put, eg + 1, dve_step)
                for k in range(4):
                    dst = OS[32 * k:32 * k + B, eg, :] if isinstance(eg, int) else \
                        OS[32 * k:32 * k + B, bass.ds(eg, 1), :].rearrange("p a d -> p (a d)")
                    nc.vector.tensor_copy(dst, PO[32 * k:32 * k + B, 0:D]).then_inc(o_got, 1)
            peeled(dve, EG, round_)

        @block.scalar
        def _(act):
            act.wait_ge(nmax_done, 1)
            nc.scalar.activation(LG[:, :], LG[:, :], ACT.Exp, bias=nmax[:, 0:1],
                                 accum_out=total[:, 0:1]).then_inc(exp_done, 1)
            act.wait_ge(zeroed, 1)

            def round_(eg):
                wait(act, t_put, eg, act_step)
                wait(act, h_put, eg + 1, act_step)
                for k in range(4):
                    nc.scalar.activation(HS[32 * k:32 * k + B, :], PH[32 * k:32 * k + B, :], ACT.Gelu)\
                        .then_inc(h_got, 1)
            peeled(act, EG, round_)

        @block.tensor
        def _(pe):
            pe.wait_ge(const_ld, 64)
            pe.wait_ge(w_done, 1)
            for n in range(NB // HC):
                if n:
                    pe.wait_ge(wt_got, n)
                for c in range(HC):
                    t = n * HC + c
                    ins = nc.tensor.transpose(TP[:, c, :], LG[:, t * P:(t + 1) * P], ident[:, :])
                ins.then_inc(wt_put, 1)
            pe.wait_ge(wt_got, NB // HC)
            for b in range(B):
                pe.wait_ge(x_ld[b % 2], 16 * (b // 2 + 1))
                for c in range(CC):
                    for t in range(NB):
                        ins = nc.tensor.matmul(PM[:, c * BE + b * NE:c * BE + (b + 1) * NE],
                                               XB[b % 2][:, t, c * P:(c + 1) * P], WTS[:, t, b * NE:(b + 1) * NE],
                                               start=(t == 0), stop=(t == NB - 1))
                ins.then_inc(xb_used, 1)

            def round_(eg, u, i):
                wait(pe, me_done, 2 * eg + 2, pe_step)
                wait(pe, h_got, 4 * eg, pe_step)
                wait(pe, w1_ld[u], 64 * i + 64, pe_step)
                for nh in range(HID // 512):
                    n = slice(nh * 512, (nh + 1) * 512)
                    for c in range(CC + 1):
                        for k in range(4):
                            lhsT, rhs = (ME[:, c, k, :], W1[u][:, k, c, n]) if c < CC else (PK[:, k, :], B1[:, n])
                            ins = nc.tensor.matmul(PH[32 * k:32 * k + B, n], lhsT, rhs,
                                                   start=(c == 0), stop=(c == CC))
                ins.then_inc(h_put, 1)
                wait(pe, h_got, 4 * eg + 4, pe_step)
                wait(pe, t_got, eg, pe_step)
                for c in range(HC):
                    ins = nc.tensor.transpose(TP[:, c, :], HS[:, c * P:(c + 1) * P], ident[:, :])
                ins.then_inc(t_put, 1)
                wait(pe, t_got, eg + 1, pe_step)
                wait(pe, o_got, 4 * eg, pe_step)
                wait(pe, w2_ld[u], 64 * i + 64, pe_step)
                for c in range(HC + 1):
                    for k in range(4):
                        lhsT, rhs = (HT[:, c, k, :], W2[u][:, k, c, :]) if c < HC else (PK[:, k, :], B2[:, :])
                        ins = nc.tensor.matmul(PO[32 * k:32 * k + B, 0:D], lhsT, rhs,
                                               start=(c == 0), stop=(c == HC))
                ins.then_inc(o_put, 1)

            def body(i):
                for u in range(2):
                    round_(2 * i + u, u, i)
            peeled(pe, EG // 2, body)

def phase_out(nc, ao_d, ow_d, ob_d, xl_d, x_d, ident_d, out_d):
    E4 = T // GT
    DH, H = DH2, HEADS2
    HPC = P // DH
    with ExitStack() as ctx:
        m = Mem(nc, ctx, "fin")
        A = [m.sb(f"A{u}", [P, H, J, DH]) for u in range(2)]
        AB = m.sb("AB", [P, J, H, DH])
        X = [m.sb(f"X{u}", [P, J, D]) for u in range(2)]
        Z = [m.sb(f"Z{u}", [P, J, D]) for u in range(2)]
        TMP = m.sb("TMP", [P, J, D])
        AT = m.sb("AT", [P, CC, GT])
        OW = m.sb("OW", [P, CC, D])
        OB = m.sb("OB", [P, D])
        stats, mv, veps, rstd = (m.sb(n, [P, J] + e) for n, e in (("stats", [6]), ("mv", [2]), ("veps", []),
                                                                  ("rstd", [])))
        nhalf = m.sb("nhalf", [P, J])
        ident = m.sb("ident", [P, P])
        PT = m.ps("PT", [P, CC, GT])
        PA = m.ps("PA", [P, J, D])
        names = ("const_ld", "half_set", "by_token", "turned", "at_ready", "a_done", "summed", "chain", "var", "rs", "xnew",
                 "pool_chain", "step", "pstep", "sstep", "pe_step")
        (const_ld, half_set, by_token, turned, at_ready, a_done, summed, chain, var, rs, xnew,
         pool_chain, step, pstep, sstep, pe_step) = (m.sem(n) for n in names)
        a_ld, x_ld, z_ld, x_st = ([m.sem(f"{n}{u}") for u in range(2)] for n in ("a_ld", "x_ld", "z_ld", "x_st"))
        block = ctx.enter_context(nc.Block())

        def nth(b, e):
            return 8 * E4 * b + 16 * (e // 2 + 1)

        @block.sync
        def _(sp):
            for dst, ap in ((ident[:, :], ident_d), (OW[:, :, :], ow_d.rearrange("(c p) n -> p c n", p=P)),
                            (OB[:, :], ob_d.partition_broadcast(P))):
                sp.dma_start(dst, ap).then_inc(const_ld, 16)

            def load(b, e):
                g, u = E4 * b + e, e % 2
                ab = group(ao_d.rearrange("(b h) p n d -> b p h n d", b=B), b)
                wait(sp, by_token, g - 1, sstep)
                sp.dma_start(A[u][:, :, :, :], ab[:, :, e * J:(e + 1) * J, :]).then_inc(a_ld[u], 16)
                wait(sp, xnew, g - 1, sstep)
                sp.dma_start(Z[u][:, :, :], group(tokens(xl_d), g)).then_inc(z_ld[u], 16)
                wait(sp, x_st[u], nth(b, e) - 16, sstep)
                sp.dma_start(X[u][:, :, :], group(tokens(x_d), g)).then_inc(x_ld[u], 16)

            def body(b):
                for e in range(E4):
                    load(b, e)
            peeled(sp, B, body)
            for u in range(2):
                sp.wait_ge(x_st[u], 8 * B * E4)

        @block.tensor
        def _(pe):
            pe.wait_ge(const_ld, 48)

            def body(b):
                for e in range(E4):
                    g, u, mm = E4 * b + e, e % 2, D >> e
                    chunks = [(c, min(P, mm - c * P)) for c in range(CC) if mm > c * P]
                    wait(pe, by_token, g + 1, pe_step)
                    wait(pe, at_ready, g, pe_step)
                    for c, k in chunks:
                        for j in range(J):
                            ins = nc.tensor.transpose(PT[:, c, j * P:(j + 1) * P],
                                                      AB[:, j, c * HPC:(c + 1) * HPC, :], ident[:, :])
                    ins.then_inc(turned, 1)
                    wait(pe, at_ready, g + 1, pe_step)
                    wait(pe, summed, g, pe_step)
                    for j in range(J):
                        for c, k in chunks:
                            ins = nc.tensor.matmul(PA[:, j, 0:mm], AT[0:k, c, j * P:(j + 1) * P], OW[0:k, c, 0:mm],
                                                   start=(c == 0), stop=(c == len(chunks) - 1))
                    ins.then_inc(a_done, 1)
            peeled(pe, B, body)

        @block.scalar
        def _(act):
            def body(b):
                for e in range(E4):
                    g, u, mm = E4 * b + e, e % 2, D >> e
                    n = max(1, mm // P)
                    wait(act, turned, g + 1)
                    wait(act, a_done, g)
                    nc.scalar.activation(AT[:, 0:n, :], PT[:, 0:n, :], ACT.Copy).then_inc(at_ready, 1)
                    if e > 0 or not isinstance(b, int) or b > 0:
                        store(g - 1, 1 - u)
            def store(g, u):
                wait(act, xnew, g + 1)
                act.dma_start(group(tokens(out_d), g), X[u][:, :, :]).then_inc(x_st[u], 16)
            peeled(act, B, body)
            store(B * E4 - 1, 1)

        @block.gpsimd
        def _(pool):
            nc.gpsimd.memset(nhalf[:, :], -0.5).then_inc(half_set, 1)
            pool.wait_ge(half_set, 1)

            def by_tokens(b, e):
                g, u = E4 * b + e, e % 2
                wait(pool, turned, g)
                wait(pool, a_ld[u], nth(b, e), pstep)
                nc.gpsimd.tensor_copy(AB[:, :, :, :].rearrange("p j h d -> p h j d"), A[u][:, :, :, :])\
                    .then_inc(by_token, 1)

            def body(b):
                for e in range(E4):
                    g = E4 * b + e
                    if e == 0 and isinstance(b, int) and b == 0:
                        by_tokens(b, e)
                    if following(b, e, E4):
                        by_tokens(*following(b, e, E4))
                    wait(pool, var, g + 1, pstep)
                    nc.gpsimd.tensor_scalar(veps[:, :], mv[:, :, 1], EPS, None, ALU.add).then_inc(pool_chain, 1)
                    wait(pool, pool_chain, g + 1)
                    nc.gpsimd.tensor_tensor(rstd[:, :], veps[:, :], nhalf[:, :], ALU.pow).then_inc(rs, 1)
            peeled(pool, B, body, last=True)

        @block.vector
        def _(dve):
            ch = Chain(dve, chain, 3 * E4, step)
            dve.wait_ge(const_ld, 48)

            def body(b):
                ch.start(b)
                for e in range(E4):
                    g, u, mm = E4 * b + e, e % 2, D >> e
                    wait(dve, z_ld[u], nth(b, e))
                    ch.link(nc.vector.tensor_tensor(Z[u][:, :, 0:mm], Z[u][:, :, 0:mm],
                                                    OB[:, 0:mm].unsqueeze(1).to_broadcast([P, J, mm]), ALU.add))
                    wait(dve, a_done, g + 1)
                    nc.vector.tensor_tensor(Z[u][:, :, 0:mm], Z[u][:, :, 0:mm], PA[:, :, 0:mm],
                                            ALU.add).then_inc(summed, 1)
                    wait(dve, summed, g + 1, step)
                    ln_stats(nc, ch, Z[u], stats, mv, var)
                    wait(dve, rs, g + 1)
                    ch.link(ln_apply(nc, Z[u], mv, rstd, TMP))
                    wait(dve, x_ld[u], nth(b, e))
                    nc.vector.tensor_tensor(X[u][:, :, :], X[u][:, :, :], TMP[:, :, :], ALU.add).then_inc(xnew, 1)
                ch.end()
            peeled(dve, B, body)


def sandwich(nc, d, out_d):
    def dram(name, shape):
        return nc.dram_tensor(name, shape, F32, kind="Internal").ap()
    xnT = dram("xnT", [CC, P, TOK])
    ycat = dram("ycat", [2 * CC, P, TOK])
    x1, xn2, x2, x3, xl = (dram(n, [TOK, D]) for n in ("x1", "xn2", "x2", "x3", "xl"))
    logits, routed = (dram(n, [B, EXPERTS, T]) for n in ("logits", "routed"))
    expert_out = dram("expert_out", [B, EXPERTS, D])
    qkv1 = dram("qkv1", [B * HEADS1, P, 3, T // P, DH1])
    ao1 = dram("ao1", [B * HEADS1, P, T // P, DH1])
    qkv2 = dram("qkv2", [B * HEADS2, P, 3, T // P, DH2])
    ao2 = dram("ao2", [B * HEADS2, P, T // P, DH2])
    ident = d["ident"]

    phase_norm_x(nc, tokens(d["x"]), ident, xnT)
    phase_wkv(nc, xnT, d["rkv_w"], d["decay"], d["first"], ycat)
    phase_rows(nc, "r2", "scan", (ycat, d["out_w"]), d["x"], x1, ident,
               "gate", (d["gate_w"], d["gate_b"], logits), xn_d=xn2)
    phase_experts(nc, logits, xn2, d["w1"], d["w2"], d["pick"], ident, routed, expert_out)
    phase_rows(nc, "r4", "experts", (routed, expert_out), x1, x2, ident, "rope", (d["wqkv1"], d["rope"], qkv1))
    phase_attention(nc, "at1", HEADS1, DH1, qkv1, ao1, ident, d["sel1"])
    phase_rows(nc, "r6", "heads", (ao1,), x2, x3, ident,
               "sliced", (d["wqkv2"], d["bias2"], d["norm_w"], d["norm_b"], qkv2), xn_d=xl)
    phase_attention(nc, "at2", HEADS2, DH2, qkv2, ao2, ident, d["sel2"])
    phase_out(nc, ao2, d["o_w"], d["o_b"], xl, x3, ident, out_d)


def kernel(**inputs):
    import numpy as _np
    import concourse.bacc as _bacc
    from concourse.bass_utils import run_bass_kernel_spmd as _run

    a = {k: _np.asarray(v) for k, v in inputs.items()}

    def columns(name):
        return _np.stack([a[name], a[name + "_rev"]]).reshape(2 * CC, P).T

    def selector(dh):
        width = 32 if dh + 1 <= 32 else 64
        return (_np.arange(P)[:, None] % width == _np.arange(dh + 1)[None, :]).astype(_np.float32)

    freq = (1.0 / 10000.0 ** (_np.arange(0, DH1, 2, dtype=_np.float32) / DH1)).astype(_np.float32)
    angle = _np.outer(_np.arange(T, dtype=_np.float32), freq)
    rope = _np.stack([_np.cos(angle), _np.sin(angle)], 1)
    rope = _np.stack([rope * DH1 ** -0.5, rope], 2).reshape(T // P, P, 2, 2, DH1 // 2)

    arrays = {
        "x": a["L0_attn_x"].reshape(TOK, D),
        "rkv_w": a["L0_attn_rkv_w"].T,
        "decay": columns("L0_attn_time_decay"),
        "first": columns("L0_attn_time_first"),
        "out_w": a["L0_attn_out_w"].T,
        "gate_w": a["L0_ffn_gate_w"].T,
        "gate_b": a["L0_ffn_gate_b"].reshape(EXPERTS, 1),
        "w1": a["L0_ffn_w1"],
        "w2": a["L0_ffn_w2"],
        "wqkv1": _np.concatenate([a["L1_attn_wq"].T, a["L1_attn_wk"].T, a["L1_attn_wv"].T], 1),
        "wqkv2": _np.concatenate([a["L1_ffn_q_w"].T, a["L1_ffn_k_w"].T, a["L1_ffn_v_w"].T], 1),
        "bias2": _np.stack([a["L1_ffn_q_b"], a["L1_ffn_k_b"], a["L1_ffn_v_b"]]),
        "norm_w": a["L1_ffn_norm_w"],
        "norm_b": a["L1_ffn_norm_b"],
        "o_w": a["L1_ffn_o_w"].T,
        "o_b": a["L1_ffn_o_b"],
        "ident": _np.eye(P, dtype=_np.float32),
        "pick": _np.repeat(_np.eye(EXPERTS, dtype=_np.float32)[:, :, None], B, axis=2),
        "rope": rope.transpose(1, 0, 2, 3, 4).astype(_np.float32),
        "sel1": selector(DH1),
        "sel2": selector(DH2),
    }
    nc = _bacc.Bacc("TRN2", target_bir_lowering=False, num_devices=1)
    feed, views = {}, {}
    for name, v in arrays.items():
        feed[f"in_{name}"] = _np.ascontiguousarray(v)
        views[name] = nc.dram_tensor(f"in_{name}", v.shape, F32, kind="ExternalInput").ap()
    out_d = nc.dram_tensor("out_0", (TOK, D), F32, kind="ExternalOutput").ap()
    sandwich(nc, views, out_d)
    result = _run(nc, [feed], core_ids=[0]).results[0]["out_0"]
    return result.reshape(B, T, D)
```
